# Optimizing a Trainium2 kernel written in Bass

```python
import numpy as np
import jax
import jax.numpy as jnp

def _softmax(x, axis=-1):
    return jax.nn.softmax(x, axis=axis)

def _gelu(x):
    return jax.nn.gelu(x, approximate=True)

def _silu(x):
    return jax.nn.silu(x)

def _sigmoid(x):
    return jax.nn.sigmoid(x)

def _layernorm(x, axis=-1, eps=1e-05):
    m = jnp.mean(x, axis=axis, keepdims=True)
    v = jnp.var(x, axis=axis, keepdims=True)
    return (x - m) / jnp.sqrt(v + eps)

def _scatter_add(tgt, idx, src, axis=0):
    return tgt.at[idx].add(src)

def _segment_sum(src, seg, n):
    return jax.ops.segment_sum(src, seg, n)
kernel_name = 'mk_dlrm_tower_d1_rec_r8_dd72c4'

def setup_inputs(seed: int=0):
    np.random.seed(seed)
    _w = jnp.asarray

    def _rec_inputs():
        import jax
        import jax.numpy as jnp
        _tk = jax.random.key(seed)
        ids = jnp.stack([jax.random.randint(jax.random.fold_in(_tk, 200 + f), (512,), 0, v, jnp.int32) for f, v in enumerate([125000, 1000, 1000, 1250, 1250, 1000, 1000, 12500, 12500, 1250, 1000, 1000, 1250, 1250, 1000, 12500, 1250, 1250, 12500, 1000, 12500, 1250, 12500, 1250, 12500, 1000])], axis=1)
        tbl_0 = 0.05 * jax.random.normal(jax.random.fold_in(_tk, 500 + 0), (125000, 128), jnp.float32)
        tbl_1 = 0.05 * jax.random.normal(jax.random.fold_in(_tk, 500 + 1), (1000, 128), jnp.float32)
        tbl_2 = 0.05 * jax.random.normal(jax.random.fold_in(_tk, 500 + 2), (1000, 128), jnp.float32)
        tbl_3 = 0.05 * jax.random.normal(jax.random.fold_in(_tk, 500 + 3), (1250, 128), jnp.float32)
        tbl_4 = 0.05 * jax.random.normal(jax.random.fold_in(_tk, 500 + 4), (1250, 128), jnp.float32)
        tbl_5 = 0.05 * jax.random.normal(jax.random.fold_in(_tk, 500 + 5), (1000, 128), jnp.float32)
        tbl_6 = 0.05 * jax.random.normal(jax.random.fold_in(_tk, 500 + 6), (1000, 128), jnp.float32)
        tbl_7 = 0.05 * jax.random.normal(jax.random.fold_in(_tk, 500 + 7), (12500, 128), jnp.float32)
        tbl_8 = 0.05 * jax.random.normal(jax.random.fold_in(_tk, 500 + 8), (12500, 128), jnp.float32)
        tbl_9 = 0.05 * jax.random.normal(jax.random.fold_in(_tk, 500 + 9), (1250, 128), jnp.float32)
        tbl_10 = 0.05 * jax.random.normal(jax.random.fold_in(_tk, 500 + 10), (1000, 128), jnp.float32)
        tbl_11 = 0.05 * jax.random.normal(jax.random.fold_in(_tk, 500 + 11), (1000, 128), jnp.float32)
        tbl_12 = 0.05 * jax.random.normal(jax.random.fold_in(_tk, 500 + 12), (1250, 128), jnp.float32)
        tbl_13 = 0.05 * jax.random.normal(jax.random.fold_in(_tk, 500 + 13), (1250, 128), jnp.float32)
        tbl_14 = 0.05 * jax.random.normal(jax.random.fold_in(_tk, 500 + 14), (1000, 128), jnp.float32)
        tbl_15 = 0.05 * jax.random.normal(jax.random.fold_in(_tk, 500 + 15), (12500, 128), jnp.float32)
        tbl_16 = 0.05 * jax.random.normal(jax.random.fold_in(_tk, 500 + 16), (1250, 128), jnp.float32)
        tbl_17 = 0.05 * jax.random.normal(jax.random.fold_in(_tk, 500 + 17), (1250, 128), jnp.float32)
        tbl_18 = 0.05 * jax.random.normal(jax.random.fold_in(_tk, 500 + 18), (12500, 128), jnp.float32)
        tbl_19 = 0.05 * jax.random.normal(jax.random.fold_in(_tk, 500 + 19), (1000, 128), jnp.float32)
        tbl_20 = 0.05 * jax.random.normal(jax.random.fold_in(_tk, 500 + 20), (12500, 128), jnp.float32)
        tbl_21 = 0.05 * jax.random.normal(jax.random.fold_in(_tk, 500 + 21), (1250, 128), jnp.float32)
        tbl_22 = 0.05 * jax.random.normal(jax.random.fold_in(_tk, 500 + 22), (12500, 128), jnp.float32)
        tbl_23 = 0.05 * jax.random.normal(jax.random.fold_in(_tk, 500 + 23), (1250, 128), jnp.float32)
        tbl_24 = 0.05 * jax.random.normal(jax.random.fold_in(_tk, 500 + 24), (12500, 128), jnp.float32)
        tbl_25 = 0.05 * jax.random.normal(jax.random.fold_in(_tk, 500 + 25), (1000, 128), jnp.float32)
        _rk = jax.random.fold_in(_tk, 7)
        r_dense_x = -0.000514642 + 1.00011 * jax.random.normal(jax.random.fold_in(_rk, 101), (512, 128), jnp.float32)
        W_top1 = 0.0456912 * jax.random.normal(jax.random.fold_in(_tk, 801), (479, 512), jnp.float32)
        W_top2 = 0.0441942 * jax.random.normal(jax.random.fold_in(_tk, 802), (512, 256), jnp.float32)
        W_top3 = 0.0625 * jax.random.normal(jax.random.fold_in(_tk, 803), (256, 1), jnp.float32)
        b_top1 = jnp.zeros((512,), jnp.float32)
        b_top2 = jnp.zeros((256,), jnp.float32)
        return (r_dense_x, ids, tbl_0, tbl_1, tbl_2, tbl_3, tbl_4, tbl_5, tbl_6, tbl_7, tbl_8, tbl_9, tbl_10, tbl_11, tbl_12, tbl_13, tbl_14, tbl_15, tbl_16, tbl_17, tbl_18, tbl_19, tbl_20, tbl_21, tbl_22, tbl_23, tbl_24, tbl_25, W_top1, b_top1, W_top2, b_top2, W_top3)
    r_dense_x, ids, tbl_0, tbl_1, tbl_2, tbl_3, tbl_4, tbl_5, tbl_6, tbl_7, tbl_8, tbl_9, tbl_10, tbl_11, tbl_12, tbl_13, tbl_14, tbl_15, tbl_16, tbl_17, tbl_18, tbl_19, tbl_20, tbl_21, tbl_22, tbl_23, tbl_24, tbl_25, W_top1, b_top1, W_top2, b_top2, W_top3 = _rec_inputs()

    def _L0_rec_setup():
        import jax, jax.numpy as jnp
        import numpy as np
        F = 26
        D = 128
        B = 2048
        _TRIU_I, _TRIU_J = np.triu_indices(F + 1, k=1)
        _TRIU_I = jnp.asarray(_TRIU_I)
        _TRIU_J = jnp.asarray(_TRIU_J)
        key = jax.random.key(seed)
        k1, k2 = jax.random.split(key)
        sparse_x = jax.random.normal(k1, (B, F, D), dtype=jnp.float32)
        dense_x = jax.random.normal(k2, (B, D), dtype=jnp.float32)
        return {'sparse_x': sparse_x, 'dense_x': dense_x}
    _L0_rec_all = _L0_rec_setup()
    _L0_rec_in = {k: v for k, v in _L0_rec_all.items() if k in ()}
    del _L0_rec_all
    return {'r_dense_x': r_dense_x, 'ids': ids, 'tbl_0': tbl_0, 'tbl_1': tbl_1, 'tbl_2': tbl_2, 'tbl_3': tbl_3, 'tbl_4': tbl_4, 'tbl_5': tbl_5, 'tbl_6': tbl_6, 'tbl_7': tbl_7, 'tbl_8': tbl_8, 'tbl_9': tbl_9, 'tbl_10': tbl_10, 'tbl_11': tbl_11, 'tbl_12': tbl_12, 'tbl_13': tbl_13, 'tbl_14': tbl_14, 'tbl_15': tbl_15, 'tbl_16': tbl_16, 'tbl_17': tbl_17, 'tbl_18': tbl_18, 'tbl_19': tbl_19, 'tbl_20': tbl_20, 'tbl_21': tbl_21, 'tbl_22': tbl_22, 'tbl_23': tbl_23, 'tbl_24': tbl_24, 'tbl_25': tbl_25, 'W_top1': W_top1, 'b_top1': b_top1, 'W_top2': W_top2, 'b_top2': b_top2, 'W_top3': W_top3}

def reference(r_dense_x, ids, tbl_0, tbl_1, tbl_2, tbl_3, tbl_4, tbl_5, tbl_6, tbl_7, tbl_8, tbl_9, tbl_10, tbl_11, tbl_12, tbl_13, tbl_14, tbl_15, tbl_16, tbl_17, tbl_18, tbl_19, tbl_20, tbl_21, tbl_22, tbl_23, tbl_24, tbl_25, W_top1, b_top1, W_top2, b_top2, W_top3):
    import jax
    import jax.numpy as jnp

    def _L0_rec_ref(sparse_x, dense_x):
        import jax, jax.numpy as jnp
        import numpy as np
        F = 26
        D = 128
        B = 2048
        _TRIU_I, _TRIU_J = np.triu_indices(F + 1, k=1)
        _TRIU_I = jnp.asarray(_TRIU_I)
        _TRIU_J = jnp.asarray(_TRIU_J)
        combined = jnp.concatenate([sparse_x, dense_x[:, None, :]], axis=1)
        interact = jnp.einsum('bfd,bgd->bfg', combined, combined)
        return interact[:, _TRIU_I, _TRIU_J]
    e = jnp.stack([tbl_0[ids[:, 0]], tbl_1[ids[:, 1]], tbl_2[ids[:, 2]], tbl_3[ids[:, 3]], tbl_4[ids[:, 4]], tbl_5[ids[:, 5]], tbl_6[ids[:, 6]], tbl_7[ids[:, 7]], tbl_8[ids[:, 8]], tbl_9[ids[:, 9]], tbl_10[ids[:, 10]], tbl_11[ids[:, 11]], tbl_12[ids[:, 12]], tbl_13[ids[:, 13]], tbl_14[ids[:, 14]], tbl_15[ids[:, 15]], tbl_16[ids[:, 16]], tbl_17[ids[:, 17]], tbl_18[ids[:, 18]], tbl_19[ids[:, 19]], tbl_20[ids[:, 20]], tbl_21[ids[:, 21]], tbl_22[ids[:, 22]], tbl_23[ids[:, 23]], tbl_24[ids[:, 24]], tbl_25[ids[:, 25]]], axis=1)
    z = _L0_rec_ref(e, r_dense_x)
    z = z.reshape(z.shape[0], -1)
    h = jnp.concatenate([z, r_dense_x], axis=1)
    h = jnp.maximum(h @ W_top1 + b_top1, 0.0)
    h = jnp.maximum(h @ W_top2 + b_top2, 0.0)
    y = h @ W_top3
    return y

_drawn_inputs = setup_inputs


def setup_inputs(seed=0):
    import zlib

    import numpy as np

    out = dict(_drawn_inputs(seed))
    spreads = {'b_top1': (0.0, 0.1), 'b_top2': (0.0, 0.1)}
    factors = {}
    for name, (base, spread) in spreads.items():
        noise = np.random.default_rng([zlib.crc32(name.encode()), seed]).standard_normal(out[name].shape)
        drawn = base * np.exp(spread * noise) if base else spread * noise
        out[name] = jnp.asarray(drawn.astype(out[name].dtype))
    for name, factor in factors.items():
        out[name] = (out[name] * factor).astype(out[name].dtype)
    return out
```

```python
from contextlib import ExitStack

import concourse.bass as bass
from concourse import mybir

F32 = mybir.dt.float32
I32 = mybir.dt.int32
ACT = mybir.ActivationFunctionType
ALU = mybir.AluOpType

P = 128
D = 128
TABLES = 26
DENSE = TABLES
SLOTS = 32
GROUP = P // SLOTS
J = TABLES
JR = 4
JB = -(-J // JR)
FIRSTS = [min(JR * jb + JR, J) for jb in range(JB)]
SLOT0 = [sum(FIRSTS[:jb]) for jb in range(JB)]
NSLOT = sum(FIRSTS)
TURN = 4
TURNS = -(-TABLES // TURN)
BANK = 512


def dlrm_tower(nc, ids, tables, dense_t, w1_pairs, w1_dense, b1, w2, b2, w3, eye, out):
    batch = ids.shape[0]
    tiles = batch // P
    groups = P // GROUP
    per_bank = BANK // (GROUP * J)
    dot_banks = groups // per_bank
    n1, n2 = w1_dense.shape[1], w2.shape[2]
    m1, m2 = n1 // P, n2 // P
    DOTB = 3

    ctx = ExitStack()
    with ctx:
        def sb(name, shape, dt=F32):
            return ctx.enter_context(nc.sbuf_tensor(name, shape, dt))

        def sem(name):
            return ctx.enter_context(nc.semaphore(name))

        ids_sb = sb("ids_sb", [P, tiles, TABLES], I32)
        rows = sb("rows", [P, tiles, TABLES, D])
        columns = sb("columns", [P, tiles, P, SLOTS])
        dots = sb("dots", [P, 2, JB * JR, groups])
        pairs_by_sample = sb("pairs_by_sample", [P, GROUP, NSLOT])
        pairs = sb("pairs", [NSLOT, GROUP, JR, groups])
        h1 = sb("h1", [P, m1, P])
        h2 = sb("h2", [P, m2, P])
        y_sb = sb("y_sb", [1, batch])
        dense_sb = sb("dense_sb", [P, batch])
        eye_sb = sb("eye_sb", [P, P])
        w1p = sb("w1p", [NSLOT, JR, n1])
        w1d = sb("w1d", [P, n1])
        w2_sb = sb("w2_sb", [P, m1, n2])
        w3_sb = sb("w3_sb", [P, m2])
        b1_sb = sb("b1_sb", [P, m1])
        b2_sb = sb("b2_sb", [P, m2])

        turn_ps = ctx.enter_context(nc.psum_tensor("turn_ps", [P, 2, TURN, P], F32))
        dot_ps = ctx.enter_context(nc.psum_tensor("dot_ps", [P, DOTB, BANK], F32))
        mid_ps = ctx.enter_context(nc.psum_tensor("mid_ps", [P, 2, 4, P], F32))
        end_ps = ctx.enter_context(nc.psum_tensor("end_ps", [P, 4, P], F32))

        ids_in = sem("ids_in")
        eye_in = sem("eye_in")
        dense_in = sem("dense_in")
        w1_in = sem("w1_in")
        w2_in = sem("w2_in")
        small_in = sem("small_in")
        gathered = [[sem(f"gathered_{t}_{q}") for q in range(TURNS)] for t in range(tiles)]
        zeroed = sem("zeroed")
        dense_set = sem("dense_set")
        turned = sem("turned")
        columns_set = sem("columns_set")
        dotted = sem("dotted")
        dots_set = sem("dots_set")
        dots_turned = sem("dots_turned")
        by_sample = sem("by_sample")
        pairs_turned = sem("pairs_turned")
        pairs_set = sem("pairs_set")
        h1_done = sem("h1_done")
        h1_set = sem("h1_set")
        h2_done = sem("h2_done")
        h2_set = sem("h2_set")
        y_done = sem("y_done")
        y_set = sem("y_set")
        y_out = sem("y_out")

        block = ctx.enter_context(nc.Block())

        @block.sync
        def _(sp):
            sp.dma_start(ids_sb[:, :, :], ids.rearrange("(t p) f -> p t f", p=P)).then_inc(ids_in, 16)
            sp.dma_start(eye_sb[:, :], eye).then_inc(eye_in, 16)
            sp.dma_start(dense_sb[:, :], dense_t).then_inc(dense_in, 16)
            sp.dma_start(w1p[:, :, :], w1_pairs).then_inc(w1_in, 16)
            sp.dma_start(w1d[:, :], w1_dense).then_inc(w1_in, 16)
            sp.dma_start(w2_sb[:, :, :], w2).then_inc(w2_in, 16)
            sp.dma_start(b1_sb[:, :], b1).then_inc(small_in, 16)
            sp.dma_start(b2_sb[:, :], b2).then_inc(small_in, 16)
            sp.dma_start(w3_sb[:, :], w3).then_inc(small_in, 16)
            sp.wait_ge(y_set, tiles)
            sp.dma_start(out.rearrange("b a -> a b"), y_sb[:, :]).then_inc(y_out, 16)
            sp.wait_ge(y_out, 16)

        @block.gpsimd
        def _(pool):
            pool.wait_ge(ids_in, 16)
            for t in range(tiles):
                for f in range(TABLES):
                    nc.gpsimd.indirect_dma_start(
                        out=rows[:, t, f, :], out_offset=None, in_=tables[f],
                        in_offset=bass.IndirectOffsetOnAxis(ap=ids_sb[:, t, f:f + 1], axis=0),
                    ).then_inc(gathered[t][f // TURN], 16)

        @block.tensor
        def _(pe):
            bank = 0
            dot = 0
            for t in range(tiles):
                if t == 0:
                    pe.wait_ge(eye_in, 16)
                for q in range(TURNS):
                    fs = range(q * TURN, min(q * TURN + TURN, TABLES))
                    pe.wait_ge(gathered[t][q], 16 * len(fs))
                    if bank >= 2:
                        pe.wait_ge(columns_set, bank - 1)
                    for f in fs:
                        last = nc.tensor.transpose(turn_ps[:, bank % 2, f % TURN, :], rows[:, t, f, :], eye_sb[:, :])
                    last.then_inc(turned, 1)
                    bank += 1

                if t == 0:
                    pe.wait_ge(zeroed, 2)
                pe.wait_ge(dense_set, t + 1)
                pe.wait_ge(columns_set, bank)
                for k in range(dot_banks):
                    if dot >= DOTB:
                        pe.wait_ge(dots_set, dot - DOTB + 1)
                    for c in range(per_bank):
                        g = k * per_bank + c
                        group = columns[:, t, g * GROUP:(g + 1) * GROUP, :]
                        last = nc.tensor.matmul(
                            dot_ps[:, dot % DOTB, c * GROUP * J:(c + 1) * GROUP * J],
                            group.rearrange("d s f -> d (s f)"), group[:, :, 1:1 + J],
                            start=True, stop=True)
                    last.then_inc(dotted, 1)
                    dot += 1

                if t:
                    pe.wait_ge(h1_set, m1 * t)
                pe.wait_ge(dots_set, dot)
                for jb in range(JB):
                    last = nc.tensor.transpose(
                        mid_ps[:, jb // 4, jb % 4, :],
                        dots[:, t % 2, jb * JR:(jb + 1) * JR, :].rearrange("p j g -> p (j g)"), eye_sb[:, :])
                    if jb in (3, JB - 1):
                        last.then_inc(dots_turned, 1)

                if t:
                    pe.wait_ge(y_set, t)
                pe.wait_ge(by_sample, 2 * (t + 1))
                for s in range(GROUP):
                    last = nc.tensor.transpose(end_ps[0:NSLOT, s, :], pairs_by_sample[:, s, :], eye_sb[:, :])
                last.then_inc(pairs_turned, 1)

                if t == 0:
                    pe.wait_ge(w1_in, 32)
                dense = dense_sb[:, t * P:(t + 1) * P].rearrange("d (g s) -> d s g", s=GROUP)
                for m in range(m1):
                    hidden = mid_ps[:, m // 2, m % 2, :]
                    nc.tensor.matmul(hidden, w1d[:, m * P:(m + 1) * P], dense, start=True, stop=False)
                    if m == 0:
                        pe.wait_ge(pairs_set, t + 1)
                    for jr in range(JR):
                        last = nc.tensor.matmul(hidden, w1p[:, jr, m * P:(m + 1) * P], pairs[:, :, jr, :],
                                                start=False, stop=jr == JR - 1)
                    if m % 2:
                        last.then_inc(h1_done, 1)

                if t == 0:
                    pe.wait_ge(w2_in, 16)
                for n in range(m2):
                    for m in range(m1):
                        if n == 0:
                            pe.wait_ge(h1_set, m1 * t + m + 1)
                        last = nc.tensor.matmul(end_ps[:, n, :], w2_sb[:, m, n * P:(n + 1) * P], h1[:, m, :],
                                                start=m == 0, stop=m == m1 - 1)
                last.then_inc(h2_done, 1)

                if t == 0:
                    pe.wait_ge(small_in, 48)
                pe.wait_ge(h2_set, m2 * (t + 1))
                for n in range(m2):
                    last = nc.tensor.matmul(end_ps[0:1, m2, :], w3_sb[:, n:n + 1], h2[:, n, :],
                                            start=n == 0, stop=n == m2 - 1)
                last.then_inc(y_done, 1)

        @block.scalar
        def _(act):
            bank = 0
            for t in range(tiles):
                for q in range(TURNS):
                    n = min(TURN, TABLES - q * TURN)
                    act.wait_ge(turned, bank + 1)
                    nc.scalar.activation(
                        columns[:, t, :, q * TURN:q * TURN + n].rearrange("d b f -> d f b"),
                        turn_ps[:, bank % 2, 0:n, :], ACT.Copy).then_inc(columns_set, 1)
                    bank += 1
                act.wait_ge(pairs_turned, t + 1)
                nc.scalar.activation(pairs.rearrange("p s j g -> p s (j g)"), end_ps[0:NSLOT, :, :],
                                     ACT.Copy).then_inc(pairs_set, 1)
                if t == 0:
                    act.wait_ge(small_in, 48)
                for m in range(m1):
                    if m % 2 == 0:
                        act.wait_ge(h1_done, 2 * t + m // 2 + 1)
                    nc.scalar.activation(h1[:, m, :], mid_ps[:, m // 2, m % 2, :], ACT.Relu,
                                         bias=b1_sb[:, m:m + 1]).then_inc(h1_set, 1)
                act.wait_ge(h2_done, t + 1)
                if t:
                    act.wait_ge(y_done, t)
                for n in range(m2):
                    nc.scalar.activation(h2[:, n, :], end_ps[:, n, :], ACT.Relu,
                                         bias=b2_sb[:, n:n + 1]).then_inc(h2_set, 1)

        @block.vector
        def _(dve):
            nc.vector.memset(columns[:, :, :, DENSE + 1:SLOTS], 0.0).then_inc(zeroed, 1)
            nc.vector.memset(dots[:, :, J:JB * JR, :], 0.0).then_inc(zeroed, 1)
            dve.wait_ge(dense_in, 16)
            for t in range(tiles):
                nc.vector.tensor_copy(columns[:, t, :, DENSE], dense_sb[:, t * P:(t + 1) * P]).then_inc(dense_set, 1)
            dot = 0
            for t in range(tiles):
                for k in range(dot_banks):
                    dve.wait_ge(dotted, dot + 1)
                    if t >= 2 and k == 0:
                        dve.wait_ge(dots_turned, 2 * (t - 1))
                    for s in range(GROUP):
                        lanes = slice(s * SLOTS, (s + 1) * SLOTS)
                        products = dot_ps[lanes, dot % DOTB, 0:per_bank * GROUP * J].rearrange(
                            "p (g s j) -> p g s j", s=GROUP, j=J)[:, :, s, :]
                        last = nc.vector.tensor_copy(
                            dots[lanes, t % 2, 0:J, k * per_bank:(k + 1) * per_bank].rearrange("p j g -> p g j"),
                            products)
                    last.then_inc(dots_set, 1)
                    dot += 1
                if t:
                    dve.wait_ge(pairs_turned, t)
                for jb in range(JB):
                    if jb in (0, 4):
                        dve.wait_ge(dots_turned, 2 * t + jb // 4 + 1)
                    last = nc.vector.tensor_copy(
                        pairs_by_sample[:, :, SLOT0[jb]:SLOT0[jb] + FIRSTS[jb]],
                        mid_ps[:, jb // 4, jb % 4, :].rearrange("p (s i) -> p s i", s=GROUP)[:, :, 0:FIRSTS[jb]])
                    if jb in (3, JB - 1):
                        last.then_inc(by_sample, 1)
                dve.wait_ge(y_done, t + 1)
                nc.vector.tensor_copy(y_sb[:, t * P:(t + 1) * P].rearrange("p (g s) -> p s g", s=GROUP),
                                      end_ps[0:1, m2, :].rearrange("p (s g) -> p s g", s=GROUP)).then_inc(y_set, 1)


def kernel(r_dense_x, ids, W_top1, b_top1, W_top2, b_top2, W_top3, **tables):
    import numpy as np
    import concourse.bacc as bacc
    from concourse.bass_utils import run_bass_kernel_spmd

    W_top1 = np.asarray(W_top1)
    row_of = np.zeros((TABLES + 1, TABLES + 1), np.int64)
    first, second = np.triu_indices(TABLES + 1, k=1)
    row_of[first, second] = np.arange(len(first))
    w1_pairs = np.zeros((NSLOT, JR, W_top1.shape[1]), W_top1.dtype)
    for jb in range(JB):
        for jr in range(JR):
            j = jb * JR + jr
            for i in range(min(j + 1, FIRSTS[jb]) if j < J else 0):
                w1_pairs[SLOT0[jb] + i, jr] = W_top1[row_of[i, j + 1]]

    def on_partitions(a):
        return np.asarray(a).reshape(-1, P, *np.asarray(a).shape[1:]).swapaxes(0, 1)

    arrays = {f"tbl_{f}": np.asarray(tables[f"tbl_{f}"]) for f in range(TABLES)}
    arrays |= {
        "ids": np.asarray(ids), "dense_t": np.asarray(r_dense_x).T, "w1_pairs": w1_pairs,
        "w1_dense": W_top1[len(first):], "b1": on_partitions(b_top1), "w2": on_partitions(W_top2),
        "b2": on_partitions(b_top2), "w3": on_partitions(W_top3)[:, :, 0], "eye": np.eye(P, dtype=np.float32),
    }
    arrays = {f"in_{k}": np.ascontiguousarray(a) for k, a in arrays.items()}
    nc = bacc.Bacc("TRN2", target_bir_lowering=False, num_devices=1)
    ap = {k[3:]: nc.dram_tensor(k, a.shape, mybir.dt.from_np(a.dtype), kind="ExternalInput").ap() for k, a in arrays.items()}
    out = nc.dram_tensor("out_y", (ids.shape[0], 1), F32, kind="ExternalOutput").ap()
    dlrm_tower(nc, ap["ids"], [ap[f"tbl_{f}"] for f in range(TABLES)], ap["dense_t"], ap["w1_pairs"],
               ap["w1_dense"], ap["b1"], ap["w2"], ap["b2"], ap["w3"], ap["eye"], out)
    return run_bass_kernel_spmd(nc, [arrays], core_ids=[0]).results[0]["out_y"]
```

```python
from contextlib import ExitStack

import concourse.bass as bass
from concourse import mybir

F32 = mybir.dt.float32
F32R = mybir.dt.float32r
I32 = mybir.dt.int32
ACT = mybir.ActivationFunctionType
ALU = mybir.AluOpType

P = 128
D = 128
TABLES = 26
DENSE = TABLES
SLOTS = 32
GROUP = P // SLOTS
J = TABLES
JR = 4
JB = -(-J // JR)
FIRSTS = [min(JR * jb + JR, J) for jb in range(JB)]
SLOT0 = [sum(FIRSTS[:jb]) for jb in range(JB)]
NSLOT = sum(FIRSTS)
TURN = 4
BANK = 512

ROWS1 = 1000
LOADS = 3
CH = 8
RP = ROWS1 // CH
RP16 = RP // 15 * 15
SMALL = (1, 2, 5, 6, 10, 11, 14, 19, 25)
FEATURES = [f for f in range(TABLES) if f not in SMALL] + list(SMALL) + [DENSE]

HOT_FROM = (22, 19, 19, 19)
TILES = len(HOT_FROM)
HOT = list(range(TABLES - 1, min(HOT_FROM) - 1, -1))
HOT_TILE = [next(t for t in range(TILES) if HOT_FROM[t] <= f) for f in HOT]


def turns_of(t):
    return [range(f, min(f + TURN, HOT_FROM[t])) for f in range(0, HOT_FROM[t], TURN)]


DOTS, TURN1, TURN2, LAYER1 = range(4)
BEFORE = (
    ("hththththtt", "", "h", "ht"),
    ("tttt", "t", "t", "ttt"),
    ("", "t", "t", "ttt"),
    ("", "", "", ""),
)
HOTS_FIRST = 5
HOTS_AMID = 1
HOTS_AFTER = (1, 0, 0, 0)


def fills():
    turns = [(t, q) for t in range(TILES) for q in range(len(turns_of(t)))]
    number = hot = turn = 0
    out = []
    for places in BEFORE:
        out.append([])
        for place in places:
            out[-1].append([])
            for kind in place:
                out[-1][-1].append((number, hot, None) if kind == "h" else (number, None, turns[turn]))
                hot, turn, number = hot + (kind == "h"), turn + (kind == "t"), number + 1
    assert hot == len(HOT) and turn == len(turns)
    return out


FILLS = fills()
HOT_FILL = [n for tile in FILLS for place in tile for n, hot, _ in place if hot is not None]
COMPLETE = [1 + max(n for tile in FILLS for place in tile for n, hot, turn in place
                    if (hot is not None and HOT_TILE[hot] <= t) or (turn is not None and turn[0] <= t))
            for t in range(TILES)]


def dlrm_tower(nc, ids, hot_ids, row_numbers, tables, dense_t, w1_pairs, w1_dense, b1, w2, b2, w3, eye, out):
    batch = ids.shape[0]
    tiles = batch // P
    assert tiles == TILES
    groups = P // GROUP
    per_bank = BANK // (GROUP * J)
    dot_banks = groups // per_bank
    n1, n2 = w1_dense.shape[1], w2.shape[2]
    m1, m2 = n1 // P, n2 // P
    DOTB = 2
    gather_at = [sum(HOT_FROM[:t]) for t in range(TILES)]

    ctx = ExitStack()
    with ctx:
        def sb(name, shape, dt=F32):
            return ctx.enter_context(nc.sbuf_tensor(name, shape, dt))

        def sem(name):
            return ctx.enter_context(nc.semaphore(name))

        ids_sb = sb("ids_sb", [P, tiles, TABLES], I32)
        rows = sb("rows", [P, sum(HOT_FROM), D])
        table_sb = sb("table_sb", [RP, LOADS, CH * D])
        high = sb("high", [RP, 2, CH * D], F32R)
        low = sb("low", [RP, 2, CH * D], F32R)
        hot_ids_sb = sb("hot_ids_sb", [P, LOADS, batch], I32)
        one_hot = sb("one_hot", [RP, 2, CH, batch], F32R)
        numbers = sb("numbers", [RP, CH])
        columns = sb("columns", [P, tiles, P, SLOTS])
        dots = sb("dots", [P, 2, JB * JR, groups])
        pairs_by_sample = sb("pairs_by_sample", [P, GROUP, NSLOT])
        pairs = sb("pairs", [NSLOT, GROUP, JR, groups])
        h1 = sb("h1", [P, m1, P])
        h2 = sb("h2", [P, m2, P])
        y_sb = sb("y_sb", [1, batch])
        dense_sb = sb("dense_sb", [P, batch])
        eye_sb = sb("eye_sb", [P, P])
        w1p = sb("w1p", [NSLOT, JR, n1])
        w1d = sb("w1d", [P, n1])
        w2_sb = sb("w2_sb", [P, m1, n2])
        w3_sb = sb("w3_sb", [P, m2])
        b1_sb = sb("b1_sb", [P, m1])
        b2_sb = sb("b2_sb", [P, m2])

        fill_ps = ctx.enter_context(nc.psum_tensor("fill_ps", [P, 2, TURN, P], F32))
        dot_ps = ctx.enter_context(nc.psum_tensor("dot_ps", [P, DOTB, BANK], F32))
        mid_ps = ctx.enter_context(nc.psum_tensor("mid_ps", [P, 2, 4, P], F32))
        pairs_ps = ctx.enter_context(nc.psum_tensor("pairs_ps", [P, GROUP, P], F32))
        out_ps = ctx.enter_context(nc.psum_tensor("out_ps", [P, 4, P], F32))

        ids_in = sem("ids_in")
        eye_in = sem("eye_in")
        dense_in = sem("dense_in")
        w1_in = sem("w1_in")
        w2_in = sem("w2_in")
        small_in = sem("small_in")
        gathered = [[sem(f"gathered_{t}_{q}") for q in range(len(turns_of(t)))] for t in range(tiles)]
        table_in = [sem(f"table_in_{n}") for n in range(len(HOT))]
        numbers_in = sem("numbers_in")
        high_set = sem("high_set")
        low_set = sem("low_set")
        one_hot_set = sem("one_hot_set")
        zero_slots = sem("zero_slots")
        zero_dots = sem("zero_dots")
        dense_set = sem("dense_set")
        filled = sem("filled")
        columns_set = sem("columns_set")
        dotted = sem("dotted")
        dots_set_dve = sem("dots_set_dve")
        dots_set_act = sem("dots_set_act")
        dots_turned = sem("dots_turned")
        by_sample = sem("by_sample")
        pairs_turned = sem("pairs_turned")
        pairs_set = sem("pairs_set")
        h1_done = sem("h1_done")
        h1_set = sem("h1_set")
        h2_done = sem("h2_done")
        h2_set = sem("h2_set")
        y_done = sem("y_done")
        y_set = sem("y_set")
        y_out = sem("y_out")

        def diagonal(t, k, dot, s):
            lanes = slice(s * SLOTS, (s + 1) * SLOTS)
            products = dot_ps[lanes, dot % DOTB, 0:per_bank * GROUP * J].rearrange(
                "p (g s j) -> p g s j", s=GROUP, j=J)[:, :, s, :]
            kept = dots[lanes, t % 2, 0:J, k * per_bank:(k + 1) * per_bank].rearrange("p j g -> p g j")
            return kept, products

        block = ctx.enter_context(nc.Block())

        @block.sync
        def _(sp):
            sp.dma_start(ids_sb[:, :, :], ids.rearrange("(t p) f -> p t f", p=P)).then_inc(ids_in, 16)
            def load_table(n):
                if n >= LOADS:
                    sp.wait_ge(low_set, n - LOADS + 1)
                    sp.wait_ge(high_set, n - LOADS + 1)
                    sp.wait_ge(one_hot_set, CH * (n - LOADS + 1))
                sp.dma_start(hot_ids_sb[:, n % LOADS, :], hot_ids[n:n + 1, :].to_broadcast([P, batch])).then_inc(table_in[n], 16)
                table = tables[FEATURES[HOT[n]]].rearrange("(p k) d -> p (k d)", k=CH)
                sp.dma_start(table_sb[0:RP16, n % LOADS, :], table[0:RP16, :]).then_inc(table_in[n], 16)
                sp.dma_start(table_sb[RP16:RP, n % LOADS, :], table[RP16:RP, :]).then_inc(table_in[n], 16)

            sp.dma_start(numbers[:, :], row_numbers).then_inc(numbers_in, 16)
            load_table(0)
            sp.dma_start(eye_sb[:, :], eye).then_inc(eye_in, 16)
            load_table(1)
            sp.dma_start(dense_sb[:, :], dense_t).then_inc(dense_in, 16)
            sp.dma_start(b1_sb[:, :], b1).then_inc(small_in, 16)
            sp.dma_start(b2_sb[:, :], b2).then_inc(small_in, 16)
            sp.dma_start(w3_sb[:, :], w3).then_inc(small_in, 16)
            for n in range(2, len(HOT)):
                load_table(n)
                if 2 <= n < 2 + JR:
                    sp.dma_start(w1p[:, n - 2, :], w1_pairs[:, n - 2, :]).then_inc(w1_in, 16)
            sp.dma_start(w1d[:, :], w1_dense).then_inc(w1_in, 16)
            sp.dma_start(w2_sb[:, :, :], w2).then_inc(w2_in, 16)
            sp.wait_ge(y_set, tiles)
            sp.dma_start(out.rearrange("b a -> a b"), y_sb[:, :]).then_inc(y_out, 16)
            sp.wait_ge(y_out, 16)

        @block.gpsimd
        def _(pool):
            pool.wait_ge(ids_in, 16)
            for t in range(tiles):
                for slot in range(HOT_FROM[t]):
                    f = FEATURES[slot]
                    nc.gpsimd.indirect_dma_start(
                        out=rows[:, gather_at[t] + slot, :], out_offset=None, in_=tables[f],
                        in_offset=bass.IndirectOffsetOnAxis(ap=ids_sb[:, t, f:f + 1], axis=0),
                    ).then_inc(gathered[t][slot // TURN], 16)

        @block.tensor
        def _(pe):
            def fill(t, place):
                for number, hot, turn in FILLS[t][place]:
                    if number >= 2:
                        pe.wait_ge(columns_set, number - 1)
                    bank = fill_ps[:, number % 2, :, :]
                    if hot is None:
                        tile, q = turn
                        slots = turns_of(tile)[q]
                        pe.wait_ge(gathered[tile][q], 16 * len(slots))
                        for c, slot in enumerate(slots):
                            last = nc.tensor.transpose(bank[:, c, :], rows[:, gather_at[tile] + slot, :], eye_sb[:, :])
                    else:
                        first = HOT_TILE[hot]
                        for part, part_set in ((high, high_set), (low, low_set)):
                            pe.wait_ge(part_set, hot + 1)
                            for k in range(CH):
                                if part is high:
                                    pe.wait_ge(one_hot_set, CH * hot + k + 1)
                                last = nc.tensor.matmul(
                                    bank[:, first:, :].rearrange("d t b -> d (t b)"),
                                    part[:, hot % 2, k * D:(k + 1) * D], one_hot[:, hot % 2, k, first * P:],
                                    start=part is high and k == 0, stop=part is low and k == CH - 1)
                    last.then_inc(filled, 1)

            def layer2(t):
                if t == 0:
                    pe.wait_ge(w2_in, 16)
                else:
                    pe.wait_ge(y_set, t)
                for n in range(m2):
                    for m in range(m1):
                        if n == 0:
                            pe.wait_ge(h1_set, m1 * t + m + 1)
                        last = nc.tensor.matmul(out_ps[:, n, :], w2_sb[:, m, n * P:(n + 1) * P], h1[:, m, :],
                                                start=m == 0, stop=m == m1 - 1)
                last.then_inc(h2_done, 1)

            def layer3(t):
                if t == 0:
                    pe.wait_ge(small_in, 48)
                pe.wait_ge(h2_set, m2 * (t + 1))
                for n in range(m2):
                    last = nc.tensor.matmul(out_ps[0:1, m2, :], w3_sb[:, n:n + 1], h2[:, n, :],
                                            start=n == 0, stop=n == m2 - 1)
                last.then_inc(y_done, 1)

            dot = 0
            pe.wait_ge(eye_in, 16)
            for t in range(tiles):
                fill(t, DOTS)

                if t == 0:
                    pe.wait_ge(zero_slots, tiles)
                pe.wait_ge(dense_set, t + 1)
                pe.wait_ge(columns_set, COMPLETE[t])
                for k in range(dot_banks):
                    if dot >= DOTB:
                        pe.wait_ge(dots_set_dve, dot - DOTB + 1)
                        pe.wait_ge(dots_set_act, dot - DOTB + 1)
                    for c in range(per_bank):
                        g = k * per_bank + c
                        group = columns[:, t, g * GROUP:(g + 1) * GROUP, :]
                        last = nc.tensor.matmul(
                            dot_ps[:, dot % DOTB, c * GROUP * J:(c + 1) * GROUP * J],
                            group.rearrange("d s f -> d (s f)"), group[:, :, 1:1 + J],
                            start=True, stop=True)
                    last.then_inc(dotted, 1)
                    dot += 1

                if t:
                    layer2(t - 1)
                fill(t, TURN1)

                if t:
                    pe.wait_ge(h1_set, m1 * t)
                pe.wait_ge(dots_set_dve, dot)
                pe.wait_ge(dots_set_act, dot)
                if t == 0:
                    pe.wait_ge(zero_dots, 1)
                for jb in range(JB):
                    last = nc.tensor.transpose(
                        mid_ps[:, jb // 4, jb % 4, :],
                        dots[:, t % 2, jb * JR:(jb + 1) * JR, :].rearrange("p j g -> p (j g)"), eye_sb[:, :])
                    if jb in (3, JB - 1):
                        last.then_inc(dots_turned, 1)

                if t:
                    layer3(t - 1)
                fill(t, TURN2)

                pe.wait_ge(by_sample, 2 * (t + 1))
                for s in range(GROUP):
                    last = nc.tensor.transpose(pairs_ps[0:NSLOT, s, :], pairs_by_sample[:, s, :], eye_sb[:, :])
                last.then_inc(pairs_turned, 1)

                fill(t, LAYER1)

                if t == 0:
                    pe.wait_ge(w1_in, 16 * (JR + 1))
                dense = dense_sb[:, t * P:(t + 1) * P].rearrange("d (g s) -> d s g", s=GROUP)
                for m in range(m1):
                    hidden = mid_ps[:, m // 2, m % 2, :]
                    nc.tensor.matmul(hidden, w1d[:, m * P:(m + 1) * P], dense, start=True, stop=False)
                    if m == 0:
                        pe.wait_ge(pairs_set, t + 1)
                    for jr in range(JR):
                        last = nc.tensor.matmul(hidden, w1p[:, jr, m * P:(m + 1) * P], pairs[:, :, jr, :],
                                                start=False, stop=jr == JR - 1)
                    if m % 2:
                        last.then_inc(h1_done, 1)

            layer2(tiles - 1)
            layer3(tiles - 1)

        @block.scalar
        def _(act):
            def high_part(n):
                act.wait_ge(table_in[n], 48)
                if n >= 2:
                    act.wait_ge(filled, HOT_FILL[n - 2] + 1)
                nc.scalar.activation(high[:, n % 2, :], table_sb[:, n % LOADS, :], ACT.Copy).then_inc(high_set, 1)

            def fill(t, place):
                for number, hot, turn in FILLS[t][place]:
                    act.wait_ge(filled, number + 1)
                    bank = fill_ps[:, number % 2, :, :]
                    if hot is None:
                        tile, slots = turn[0], turns_of(turn[0])[turn[1]]
                        nc.scalar.activation(
                            columns[:, tile, :, slots.start:slots.stop].rearrange("d b f -> d f b"),
                            bank[:, 0:len(slots), :], ACT.Copy).then_inc(columns_set, 1)
                    else:
                        nc.scalar.activation(columns[:, HOT_TILE[hot]:, :, HOT[hot]], bank[:, HOT_TILE[hot]:, :],
                                             ACT.Copy).then_inc(columns_set, 1)
                        if hot + 2 < len(HOT):
                            high_part(hot + 2)

            high_part(0)
            act.wait_ge(eye_in, 16)
            for t in range(tiles):
                spare = columns[:, t, :, DENSE + 1:SLOTS]
                nc.scalar.activation(spare, eye_sb[:, :, None].to_broadcast(list(spare.shape)), ACT.Copy,
                                     scale=0.0).then_inc(zero_slots, 1)
            high_part(1)
            def second_hidden(t):
                act.wait_ge(h2_done, t + 1)
                if t:
                    act.wait_ge(y_done, t)
                for n in range(m2):
                    nc.scalar.activation(h2[:, n, :], out_ps[:, n, :], ACT.Relu,
                                         bias=b2_sb[:, n:n + 1]).then_inc(h2_set, 1)

            dot = 0
            for t in range(tiles):
                fill(t, DOTS)
                for k in range(dot_banks):
                    act.wait_ge(dotted, dot + 1)
                    if t >= 2 and k == 0:
                        act.wait_ge(dots_turned, 2 * (t - 1))
                    for s in range(GROUP // 2, GROUP):
                        kept, products = diagonal(t, k, dot, s)
                        last = nc.scalar.activation(kept, products, ACT.Copy)
                    last.then_inc(dots_set_act, 1)
                    dot += 1
                if t:
                    second_hidden(t - 1)
                fill(t, TURN1)
                fill(t, TURN2)
                act.wait_ge(pairs_turned, t + 1)
                nc.scalar.activation(pairs.rearrange("p s j g -> p s (j g)"), pairs_ps[0:NSLOT, :, :],
                                     ACT.Copy).then_inc(pairs_set, 1)
                fill(t, LAYER1)
                if t == 0:
                    act.wait_ge(small_in, 48)
                for m in range(m1):
                    if m % 2 == 0:
                        act.wait_ge(h1_done, 2 * t + m // 2 + 1)
                    nc.scalar.activation(h1[:, m, :], mid_ps[:, m // 2, m % 2, :], ACT.Relu,
                                         bias=b1_sb[:, m:m + 1]).then_inc(h1_set, 1)
            second_hidden(tiles - 1)

        @block.vector
        def _(dve):
            def one_hot_chunk(n, k):
                first = HOT_TILE[n] * P
                if k == 0:
                    dve.wait_ge(table_in[n], 48)
                    if n >= 2:
                        dve.wait_ge(filled, HOT_FILL[n - 2] + 1)
                made = nc.vector.tensor_scalar(one_hot[:, n % 2, k, first:], hot_ids_sb[0:RP, n % LOADS, first:],
                                               numbers[:, k:k + 1], None, ALU.is_equal)
                made.then_inc(one_hot_set, 1)

            def low_part(n):
                dve.wait_ge(high_set, n + 1)
                nc.vector.tensor_tensor(low[:, n % 2, :], table_sb[:, n % LOADS, :], high[:, n % 2, :].bitcast(F32),
                                        ALU.subtract).then_inc(low_set, 1)

            def hot_part(n):
                for k in range(CH):
                    one_hot_chunk(n, k)
                low_part(n)

            dve.wait_ge(numbers_in, 16)
            hot_part(0)
            nc.vector.memset(dots[:, :, J:JB * JR, :], 0.0).then_inc(zero_dots, 1)

            dve.wait_ge(dense_in, 16)
            for t in range(tiles):
                nc.vector.tensor_copy(columns[:, t, :, DENSE], dense_sb[:, t * P:(t + 1) * P]).then_inc(dense_set, 1)
            for n in range(1, HOTS_FIRST):
                hot_part(n)
            def outputs(t):
                dve.wait_ge(y_done, t + 1)
                nc.vector.tensor_copy(y_sb[:, t * P:(t + 1) * P].rearrange("p (g s) -> p s g", s=GROUP),
                                      out_ps[0:1, m2, :].rearrange("p (s g) -> p s g", s=GROUP)).then_inc(y_set, 1)

            assert dot_banks == CH
            hot = HOTS_FIRST
            dot = 0
            for t in range(tiles):
                for k in range(dot_banks):
                    dve.wait_ge(dotted, dot + 1)
                    if t >= 2 and k == 0:
                        dve.wait_ge(dots_turned, 2 * (t - 1))
                    for s in range(GROUP // 2):
                        kept, products = diagonal(t, k, dot, s)
                        last = nc.vector.tensor_copy(kept, products)
                    last.then_inc(dots_set_dve, 1)
                    if t == 0 and HOTS_AMID:
                        one_hot_chunk(hot, k)
                    dot += 1
                if t:
                    dve.wait_ge(pairs_turned, t)
                for jb in range(JB):
                    if jb in (0, 4):
                        dve.wait_ge(dots_turned, 2 * t + jb // 4 + 1)
                    last = nc.vector.tensor_copy(
                        pairs_by_sample[:, :, SLOT0[jb]:SLOT0[jb] + FIRSTS[jb]],
                        mid_ps[:, jb // 4, jb % 4, :].rearrange("p (s i) -> p s i", s=GROUP)[:, :, 0:FIRSTS[jb]])
                    if jb in (3, JB - 1):
                        last.then_inc(by_sample, 1)
                if t:
                    outputs(t - 1)
                if t == 0 and HOTS_AMID:
                    low_part(hot)
                    hot += 1
                for _ in range(HOTS_AFTER[t]):
                    hot_part(hot)
                    hot += 1
            outputs(tiles - 1)


def kernel(r_dense_x, ids, W_top1, b_top1, W_top2, b_top2, W_top3, **tables):
    import numpy as np
    import concourse.bacc as bacc
    from concourse.bass_utils import run_bass_kernel_spmd

    W_top1 = np.asarray(W_top1)
    row_of = np.zeros((TABLES + 1, TABLES + 1), np.int64)
    first, second = np.triu_indices(TABLES + 1, k=1)
    row_of[first, second] = row_of[second, first] = np.arange(len(first))
    w1_pairs = np.zeros((NSLOT, JR, W_top1.shape[1]), W_top1.dtype)
    for jb in range(JB):
        for jr in range(JR):
            j = jb * JR + jr
            for i in range(min(j + 1, FIRSTS[jb]) if j < J else 0):
                w1_pairs[SLOT0[jb] + i, jr] = W_top1[row_of[FEATURES[i], FEATURES[j + 1]]]

    def on_partitions(a):
        return np.asarray(a).reshape(-1, P, *np.asarray(a).shape[1:]).swapaxes(0, 1)

    arrays = {f"tbl_{f}": np.asarray(tables[f"tbl_{f}"]) for f in range(TABLES)}
    arrays |= {
        "ids": np.asarray(ids), "hot_ids": np.asarray(ids).T[[FEATURES[f] for f in HOT]],
        "row_numbers": np.arange(ROWS1, dtype=np.float32).reshape(RP, CH), "dense_t": np.asarray(r_dense_x).T, "w1_pairs": w1_pairs,
        "w1_dense": W_top1[len(first):], "b1": on_partitions(b_top1), "w2": on_partitions(W_top2),
        "b2": on_partitions(b_top2), "w3": on_partitions(W_top3)[:, :, 0], "eye": np.eye(P, dtype=np.float32),
    }
    arrays = {f"in_{k}": np.ascontiguousarray(a) for k, a in arrays.items()}
    nc = bacc.Bacc("TRN2", target_bir_lowering=False, num_devices=1)
    ap = {k[3:]: nc.dram_tensor(k, a.shape, mybir.dt.from_np(a.dtype), kind="ExternalInput").ap() for k, a in arrays.items()}
    out = nc.dram_tensor("out_y", (ids.shape[0], 1), F32, kind="ExternalOutput").ap()
    dlrm_tower(nc, ap["ids"], ap["hot_ids"], ap["row_numbers"], [ap[f"tbl_{f}"] for f in range(TABLES)], ap["dense_t"], ap["w1_pairs"],
               ap["w1_dense"], ap["b1"], ap["w2"], ap["b2"], ap["w3"], ap["eye"], out)
    return run_bass_kernel_spmd(nc, [arrays], core_ids=[0]).results[0]["out_y"]
```

```python
from contextlib import ExitStack

import concourse.bass as bass
from concourse import mybir

F32 = mybir.dt.float32
F32R = mybir.dt.float32r
BF16 = mybir.dt.bfloat16
I32 = mybir.dt.int32
ACT = mybir.ActivationFunctionType
ALU = mybir.AluOpType

P = 128
D = 128
TABLES = 26
DENSE = TABLES
SLOTS = 32
GROUP = P // SLOTS
J = DENSE + 1
JR = 3
JB = J // JR
FIRSTS = [JR * jb + JR - 1 for jb in range(JB)]
ROW0 = [sum(FIRSTS[:jb]) for jb in range(JB)]
NROW = sum(FIRSTS)
TURNED = (range(JB - 1, JB - 5, -1), range(JB - 5, JB - 9, -1), range(JB - 9, -1, -1))
TURN = 4
BANK = 512

ROWS1 = 1000
LOADS = 3
CH = 8
RP = ROWS1 // CH
RP16 = RP // 15 * 15
SMALL = (1, 2, 5, 6, 10, 11, 14, 19, 25)
FEATURES = [f for f in range(TABLES) if f not in SMALL] + list(SMALL) + [DENSE]

HOT_FROM = (21, 18, 18, 19)
TILES = len(HOT_FROM)
HOT = list(range(TABLES - 1, min(HOT_FROM) - 1, -1))
HOT_TILE = [min(t for t in range(TILES) if HOT_FROM[t] <= f) for f in HOT]
HOT_END = [1 + max(t for t in range(TILES) if HOT_FROM[t] <= f) for f in HOT]


def turns_of(t):
    return [range(f, min(f + TURN, HOT_FROM[t])) for f in range(0, HOT_FROM[t], TURN)]


DOTS, AMID1, AMID2, TURN1, TURN2, LAYER1 = range(6)
AMID = {2: AMID1, 5: AMID2}
BEFORE = (
    ("hhtththttht", "", "", "tt", "thht", "th"),
    ("", "t", "", "tt", "t", "t"),
    ("", "", "", "t", "t", "t"),
    ("tt", "", "", "", "", ""),
)
HOTS_FIRST = 6
HOTS_AMID = 1
HOTS_AFTER = (1, 0, 0, 0)
WARM_UPS = 13


def fills():
    turns = [(t, q) for t in range(TILES) for q in range(len(turns_of(t)))]
    number = hot = turn = 0
    out = []
    for places in BEFORE:
        out.append([])
        for place in places:
            out[-1].append([])
            for kind in place:
                out[-1][-1].append((number, hot, None) if kind == "h" else (number, None, turns[turn]))
                hot, turn, number = hot + (kind == "h"), turn + (kind == "t"), number + 1
    assert hot == len(HOT) and turn == len(turns)
    return out


FILLS = fills()
HOT_FILL = [n for tile in FILLS for place in tile for n, hot, _ in place if hot is not None]
COMPLETE = [1 + max(n for tile in FILLS for place in tile for n, hot, turn in place
                    if (hot is not None and HOT_TILE[hot] <= t) or (turn is not None and turn[0] <= t))
            for t in range(TILES)]
HIGH_LAG = (0, 0, 0, 1, 1, 2, 1, 0)
HIGH_AFTER = [HOT_FILL[n - 2] + HIGH_LAG[n] if n >= 2 else None for n in range(len(HOT))]


def dlrm_tower(nc, ids, hot_ids, tables, dense_t, w1_pairs, w1_dense, b1, w2, b2, w3, eye, out):
    batch = ids.shape[0]
    tiles = batch // P
    assert tiles == TILES
    groups = P // GROUP
    seconds = J - 1
    per_bank = BANK // (GROUP * seconds)
    dot_banks = groups // per_bank
    n1, n2 = w1_dense.shape[1], w2.shape[2]
    m1, m2 = n1 // P, n2 // P
    assert m2 == 2 and [len(b) for b in TURNED] == [4, 4, 1]
    DOTB = 2
    gather_at = [sum(HOT_FROM[:t]) for t in range(TILES)]

    ctx = ExitStack()
    with ctx:
        def sb(name, shape, dt=F32):
            return ctx.enter_context(nc.sbuf_tensor(name, shape, dt))

        def sem(name):
            return ctx.enter_context(nc.semaphore(name))

        ids_sb = sb("ids_sb", [P, tiles, TABLES], I32)
        rows = sb("rows", [P, sum(HOT_FROM), D])
        table_sb = sb("table_sb", [RP, LOADS, CH * D])
        high = sb("high", [RP, 2, CH * D], F32R)
        low = sb("low", [RP, 2, CH * D], F32R)
        hot_ids_sb = sb("hot_ids_sb", [P, LOADS, batch], I32)
        one_hot = sb("one_hot", [RP, 2, CH, batch], F32R)
        numbers = sb("numbers", [RP, CH])
        warm_sb = sb("warm_sb", [P, BANK], BF16)
        columns = sb("columns", [P, tiles, P, SLOTS])
        dots = sb("dots", [P, 2, J, groups])
        pairs_by_sample = sb("pairs_by_sample", [JR * groups, GROUP, NROW])
        pairs = sb("pairs", [NROW, GROUP, JR, groups])
        h1 = sb("h1", [P, m1, P])
        h2 = sb("h2", [P, m2, P])
        y_sb = sb("y_sb", [1, batch])
        dense_sb = sb("dense_sb", [P, batch])
        eye_sb = sb("eye_sb", [P, P])
        w1p = sb("w1p", [NROW, JR, n1])
        w1d = sb("w1d", [P, n1])
        w2_sb = sb("w2_sb", [P, m1, n2])
        w3_sb = sb("w3_sb", [P, m2])
        b1_sb = sb("b1_sb", [P, m1])
        b2_sb = sb("b2_sb", [P, m2])

        fill_ps = ctx.enter_context(nc.psum_tensor("fill_ps", [P, 2, TURN, P], F32))
        dot_ps = ctx.enter_context(nc.psum_tensor("dot_ps", [P, DOTB, BANK], F32))
        mid_ps = ctx.enter_context(nc.psum_tensor("mid_ps", [P, 2, 4, P], F32))
        pairs_ps = ctx.enter_context(nc.psum_tensor("pairs_ps", [P, GROUP, P], F32))
        out_ps = ctx.enter_context(nc.psum_tensor("out_ps", [P, 4, P], F32))

        warm_set = sem("warm_set")
        ids_in = sem("ids_in")
        eye_in = sem("eye_in")
        dense_in = sem("dense_in")
        w1_in = sem("w1_in")
        w2_in = sem("w2_in")
        small_in = sem("small_in")
        gathered = [[sem(f"gathered_{t}_{q}") for q in range(len(turns_of(t)))] for t in range(tiles)]
        hot_ids_in = [sem(f"hot_ids_in_{n}") for n in range(len(HOT))]
        table_in = [sem(f"table_in_{n}") for n in range(len(HOT))]
        numbers_set = sem("numbers_set")
        high_set = sem("high_set")
        low_set = sem("low_set")
        one_hot_set = sem("one_hot_set")
        zero_slots = sem("zero_slots")
        dense_set = sem("dense_set")
        filled = sem("filled")
        columns_set = sem("columns_set")
        dotted = sem("dotted")
        dots_set_dve = sem("dots_set_dve")
        dots_set_act = sem("dots_set_act")
        dots_turned = sem("dots_turned")
        by_sample_act = sem("by_sample_act")
        by_sample_dve = sem("by_sample_dve")
        pairs_turned = sem("pairs_turned")
        pairs_set = sem("pairs_set")
        h1_done = sem("h1_done")
        h1_set = sem("h1_set")
        h2_done = sem("h2_done")
        h2_set_act = sem("h2_set_act")
        h2_set_dve = sem("h2_set_dve")
        y_done = sem("y_done")
        y_set = sem("y_set")
        y_out = sem("y_out")

        def turned_dots(jb):
            bank = next(n for n, blocks in enumerate(TURNED) if jb in blocks)
            at = TURNED[bank].index(jb)
            return pairs_ps[0:JR * groups, at, :] if bank == 2 else mid_ps[0:JR * groups, bank, at, :]

        def hidden1(t, m):
            return (fill_ps if t == tiles - 1 else mid_ps)[:, m // 2, m % 2, :]

        def hidden2(n):
            return (out_ps[:, 0, :], pairs_ps[:, 0, :])[n]

        def keep_pairs(copy, jb):
            return copy(pairs_by_sample[:, :, ROW0[jb]:ROW0[jb] + FIRSTS[jb]],
                        turned_dots(jb).rearrange("p (s i) -> p s i", s=GROUP)[:, :, 0:FIRSTS[jb]])

        def diagonal(t, k, dot, s):
            lanes = slice(s * SLOTS, (s + 1) * SLOTS)
            products = dot_ps[lanes, dot % DOTB, 0:per_bank * GROUP * seconds].rearrange(
                "p (g s j) -> p g s j", s=GROUP, j=seconds)[:, :, s, :]
            kept = dots[lanes, t % 2, 1:J, k * per_bank:(k + 1) * per_bank].rearrange("p j g -> p g j")
            return kept, products

        block = ctx.enter_context(nc.Block())

        @block.sync
        def _(sp):
            sp.dma_start(ids_sb[:, :, :], ids.rearrange("(t p) f -> p t f", p=P)).then_inc(ids_in, 16)

            def load_table(n):
                if n >= LOADS:
                    sp.wait_ge(low_set, n - LOADS + 1)
                    sp.wait_ge(high_set, n - LOADS + 1)
                    sp.wait_ge(one_hot_set, CH * (n - LOADS + 1))
                sp.dma_start(hot_ids_sb[:, n % LOADS, :],
                             hot_ids[n:n + 1, :].to_broadcast([P, batch])).then_inc(hot_ids_in[n], 16)
                table = tables[FEATURES[HOT[n]]].rearrange("(p k) d -> p (k d)", k=CH)
                sp.dma_start(table_sb[0:RP16, n % LOADS, :], table[0:RP16, :]).then_inc(table_in[n], 16)
                sp.dma_start(table_sb[RP16:RP, n % LOADS, :], table[RP16:RP, :]).then_inc(table_in[n], 16)

            load_table(0)
            sp.dma_start(eye_sb[:, :], eye).then_inc(eye_in, 16)
            load_table(1)
            sp.dma_start(dense_sb[:, :], dense_t).then_inc(dense_in, 16)
            sp.dma_start(b1_sb[:, :], b1).then_inc(small_in, 16)
            sp.dma_start(b2_sb[:, :], b2).then_inc(small_in, 16)
            sp.dma_start(w3_sb[:, :], w3).then_inc(small_in, 16)
            for n in range(2, len(HOT)):
                load_table(n)
                if 2 <= n < 2 + JR:
                    sp.dma_start(w1p[:, n - 2, :], w1_pairs[:, n - 2, :]).then_inc(w1_in, 16)
            sp.dma_start(w1d[:, :], w1_dense).then_inc(w1_in, 16)
            sp.dma_start(w2_sb[:, :, :], w2).then_inc(w2_in, 16)
            sp.wait_ge(y_set, tiles)
            sp.dma_start(out.rearrange("b a -> a b"), y_sb[:, :]).then_inc(y_out, 16)
            sp.wait_ge(y_out, 16)

        @block.gpsimd
        def _(pool):
            nc.gpsimd.iota(numbers[:, :], [[1, CH]], base=0, channel_multiplier=CH,
                           allow_small_or_imprecise_dtypes=True).then_inc(numbers_set, 1)
            pool.wait_ge(ids_in, 16)
            for t in range(tiles):
                for slot in range(HOT_FROM[t]):
                    f = FEATURES[slot]
                    nc.gpsimd.indirect_dma_start(
                        out=rows[:, gather_at[t] + slot, :], out_offset=None, in_=tables[f],
                        in_offset=bass.IndirectOffsetOnAxis(ap=ids_sb[:, t, f:f + 1], axis=0),
                    ).then_inc(gathered[t][slot // TURN], 16)

        @block.tensor
        def _(pe):
            def fill(t, place):
                for number, hot, turn in FILLS[t][place]:
                    if number >= 2:
                        pe.wait_ge(columns_set, number - 1)
                    bank = fill_ps[:, number % 2, :, :]
                    if hot is None:
                        tile, q = turn
                        slots = turns_of(tile)[q]
                        pe.wait_ge(gathered[tile][q], 16 * len(slots))
                        for c, slot in enumerate(slots):
                            last = nc.tensor.transpose(bank[:, c, :], rows[:, gather_at[tile] + slot, :], eye_sb[:, :])
                    else:
                        first, end = HOT_TILE[hot], HOT_END[hot]
                        for part, part_set in ((high, high_set), (low, low_set)):
                            pe.wait_ge(part_set, hot + 1)
                            for k in range(CH):
                                if part is high:
                                    pe.wait_ge(one_hot_set, CH * hot + k + 1)
                                last = nc.tensor.matmul(
                                    bank[:, first:end, :].rearrange("d t b -> d (t b)"),
                                    part[:, hot % 2, k * D:(k + 1) * D], one_hot[:, hot % 2, k, first * P:end * P],
                                    start=part is high and k == 0, stop=part is low and k == CH - 1)
                    last.then_inc(filled, 1)

            def layer1_dense(t):
                dense = dense_sb[:, t * P:(t + 1) * P].rearrange("d (g s) -> d s g", s=GROUP)
                for m in range(m1):
                    nc.tensor.matmul(hidden1(t, m), w1d[:, m * P:(m + 1) * P], dense,
                                     start=m % 2 == 0, stop=False, skip_group_check=True)

            def layer2(t):
                if t == 0:
                    pe.wait_ge(w2_in, 16)
                else:
                    pe.wait_ge(y_set, t)
                for half in range(2):
                    for n in range(m2):
                        for m in range(half * m1 // 2, (half + 1) * m1 // 2):
                            if n == 0:
                                pe.wait_ge(h1_set, m1 * t + m + 1)
                            last = nc.tensor.matmul(hidden2(n), w2_sb[:, m, n * P:(n + 1) * P], h1[:, m, :],
                                                    start=m == 0, stop=m == m1 - 1)
                        if half:
                            last.then_inc(h2_done, 1)

            def layer3(t):
                if t == 0:
                    pe.wait_ge(small_in, 48)
                pe.wait_ge(h2_set_act, t + 1)
                pe.wait_ge(h2_set_dve, t + 1)
                for n in range(m2):
                    last = nc.tensor.matmul(out_ps[0:1, m2, :], w3_sb[:, n:n + 1], h2[:, n, :],
                                            start=n == 0, stop=n == m2 - 1)
                last.then_inc(y_done, 1)

            pe.wait_ge(warm_set, 1)
            for _ in range(WARM_UPS):
                nc.tensor.matmul(out_ps.rearrange("p a b -> p (a b)"), warm_sb[:, 0:P], warm_sb[:, :],
                                 start=True, stop=True)

            dot = 0
            pe.wait_ge(eye_in, 16)
            for t in range(tiles):
                fill(t, DOTS)
                if t == tiles - 1:
                    layer2(t - 1)

                if t == 0:
                    pe.wait_ge(zero_slots, tiles + 1)
                pe.wait_ge(dense_set, t + 1)
                pe.wait_ge(columns_set, COMPLETE[t])
                for k in range(dot_banks):
                    if dot >= DOTB:
                        pe.wait_ge(dots_set_dve, dot - DOTB + 1)
                        pe.wait_ge(dots_set_act, dot - DOTB + 1)
                    for c in range(per_bank):
                        g = k * per_bank + c
                        group = columns[:, t, g * GROUP:(g + 1) * GROUP, :]
                        last = nc.tensor.matmul(
                            dot_ps[:, dot % DOTB, c * GROUP * seconds:(c + 1) * GROUP * seconds],
                            group.rearrange("d s f -> d (s f)"), group[:, :, 1:J],
                            start=True, stop=True)
                    last.then_inc(dotted, 1)
                    dot += 1
                    if k in AMID:
                        fill(t, AMID[k])

                if 0 < t < tiles - 1:
                    layer2(t - 1)
                fill(t, TURN1)

                if t == tiles - 1:
                    layer1_dense(t)

                if t:
                    pe.wait_ge(h1_set, m1 * t)
                    pe.wait_ge(h2_set_dve, t)
                pe.wait_ge(dots_set_dve, dot)
                pe.wait_ge(dots_set_act, dot)
                for blocks in TURNED:
                    for jb in blocks:
                        last = nc.tensor.transpose(
                            turned_dots(jb),
                            dots[:, t % 2, jb * JR:(jb + 1) * JR, :].rearrange("p j g -> p (j g)"), eye_sb[:, :])
                    last.then_inc(dots_turned, 1)

                if t:
                    layer3(t - 1)
                fill(t, TURN2)

                pe.wait_ge(by_sample_act, t + 1)
                pe.wait_ge(by_sample_dve, t + 1)
                for s in range(GROUP):
                    last = nc.tensor.transpose(pairs_ps[0:NROW, s, 0:JR * groups], pairs_by_sample[:, s, :],
                                               eye_sb[0:JR * groups, 0:JR * groups])
                last.then_inc(pairs_turned, 1)

                fill(t, LAYER1)

                if t == 0:
                    pe.wait_ge(w1_in, 16 * (JR + 1))
                if t < tiles - 1:
                    layer1_dense(t)
                pe.wait_ge(pairs_set, t + 1)
                for m in range(m1):
                    for jr in range(JR):
                        last = nc.tensor.matmul(hidden1(t, m), w1p[:, jr, m * P:(m + 1) * P],
                                                pairs[:, :, jr, :], start=False, stop=jr == JR - 1,
                                                skip_group_check=True)
                    if m % 2:
                        last.then_inc(h1_done, 1)

            layer2(tiles - 1)
            layer3(tiles - 1)

        @block.scalar
        def _(act):
            def high_part(n):
                act.wait_ge(table_in[n], 32)
                if n >= 2:
                    act.wait_ge(filled, HOT_FILL[n - 2] + 1)
                nc.scalar.activation(high[:, n % 2, :], table_sb[:, n % LOADS, :], ACT.Copy).then_inc(high_set, 1)

            def fill(t, place):
                for number, hot, turn in FILLS[t][place]:
                    act.wait_ge(filled, number + 1)
                    bank = fill_ps[:, number % 2, :, :]
                    if hot is None:
                        tile, slots = turn[0], turns_of(turn[0])[turn[1]]
                        nc.scalar.activation(
                            columns[:, tile, :, slots.start:slots.stop].rearrange("d b f -> d f b"),
                            bank[:, 0:len(slots), :], ACT.Copy).then_inc(columns_set, 1)
                    else:
                        picked = slice(HOT_TILE[hot], HOT_END[hot])
                        nc.scalar.activation(columns[:, picked, :, HOT[hot]], bank[:, picked, :],
                                             ACT.Copy).then_inc(columns_set, 1)
                    if number in HIGH_AFTER:
                        high_part(HIGH_AFTER.index(number))

            high_part(0)
            high_part(1)
            act.wait_ge(eye_in, 16)
            for t in range(tiles):
                spare = columns[:, t, :, DENSE + 1:SLOTS]
                nc.scalar.activation(spare, eye_sb[:, :, None].to_broadcast(list(spare.shape)), ACT.Copy,
                                     scale=0.0).then_inc(zero_slots, 1)
            nc.scalar.activation(dots[:, :, 0, :], eye_sb[:, 0:2 * groups].rearrange("p (h g) -> p h g", h=2),
                                 ACT.Copy, scale=0.0).then_inc(zero_slots, 1)

            def second_hidden(t):
                act.wait_ge(h2_done, m2 * t + 1)
                if t:
                    act.wait_ge(y_done, t)
                nc.scalar.activation(h2[:, 0, :], hidden2(0), ACT.Relu, bias=b2_sb[:, 0:1]).then_inc(h2_set_act, 1)

            dot = 0
            for t in range(tiles):
                fill(t, DOTS)
                if t == tiles - 1:
                    second_hidden(t - 1)
                for k in range(dot_banks):
                    act.wait_ge(dotted, dot + 1)
                    if t >= 2 and k == 0:
                        act.wait_ge(dots_turned, len(TURNED) * (t - 1))
                    for s in range(GROUP // 2, GROUP):
                        kept, products = diagonal(t, k, dot, s)
                        last = nc.scalar.activation(kept, products, ACT.Copy)
                    last.then_inc(dots_set_act, 1)
                    dot += 1
                    if k in AMID:
                        fill(t, AMID[k])
                if 0 < t < tiles - 1:
                    second_hidden(t - 1)
                fill(t, TURN1)
                act.wait_ge(dots_turned, len(TURNED) * t + 1)
                for jb in TURNED[0]:
                    last = keep_pairs(lambda kept, pairs: nc.scalar.activation(kept, pairs, ACT.Copy), jb)
                last.then_inc(by_sample_act, 1)
                fill(t, TURN2)
                act.wait_ge(pairs_turned, t + 1)
                nc.scalar.activation(pairs.rearrange("p s j g -> p s (j g)"), pairs_ps[0:NROW, :, 0:JR * groups],
                                     ACT.Copy).then_inc(pairs_set, 1)
                fill(t, LAYER1)
                if t == 0:
                    act.wait_ge(small_in, 48)
                for m in range(m1):
                    if m % 2 == 0:
                        act.wait_ge(h1_done, 2 * t + m // 2 + 1)
                    nc.scalar.activation(h1[:, m, :], hidden1(t, m), ACT.Relu,
                                         bias=b1_sb[:, m:m + 1]).then_inc(h1_set, 1)
            second_hidden(tiles - 1)

        @block.vector
        def _(dve):
            def one_hot_chunk(n, k):
                samples = slice(HOT_TILE[n] * P, HOT_END[n] * P)
                if k == 0:
                    dve.wait_ge(hot_ids_in[n], 16)
                    if n >= 2:
                        dve.wait_ge(filled, HOT_FILL[n - 2] + 1)
                made = nc.vector.tensor_scalar(one_hot[:, n % 2, k, samples], hot_ids_sb[0:RP, n % LOADS, samples],
                                               numbers[:, k:k + 1], None, ALU.is_equal)
                made.then_inc(one_hot_set, 1)

            def low_part(n):
                dve.wait_ge(high_set, n + 1)
                nc.vector.tensor_tensor(low[:, n % 2, :], table_sb[:, n % LOADS, :], high[:, n % 2, :].bitcast(F32),
                                        ALU.subtract).then_inc(low_set, 1)

            def hot_part(n):
                for k in range(CH):
                    one_hot_chunk(n, k)
                low_part(n)

            nc.vector.memset(warm_sb[:, :], 0.0).then_inc(warm_set, 1)
            dve.wait_ge(numbers_set, 1)
            for n in range(HOTS_FIRST - 1):
                hot_part(n)
            dve.wait_ge(dense_in, 16)
            for t in range(tiles):
                nc.vector.tensor_copy(columns[:, t, :, DENSE], dense_sb[:, t * P:(t + 1) * P]).then_inc(dense_set, 1)
            hot_part(HOTS_FIRST - 1)

            def second_hidden(t):
                dve.wait_ge(h2_done, m2 * (t + 1))
                nc.vector.tensor_scalar(h2[:, 1, :], hidden2(1), b2_sb[:, 1:2], 0.0, ALU.add, ALU.max)\
                    .then_inc(h2_set_dve, 1)

            def outputs(t):
                dve.wait_ge(y_done, t + 1)
                nc.vector.tensor_copy(y_sb[:, t * P:(t + 1) * P].rearrange("p (g s) -> p s g", s=GROUP),
                                      out_ps[0:1, m2, :].rearrange("p (s g) -> p s g", s=GROUP)).then_inc(y_set, 1)

            assert dot_banks == CH
            dve.wait_ge(small_in, 48)
            hot = HOTS_FIRST
            dot = 0
            for t in range(tiles):
                if t == tiles - 1:
                    second_hidden(t - 1)
                for k in range(dot_banks):
                    dve.wait_ge(dotted, dot + 1)
                    if t >= 2 and k == 0:
                        dve.wait_ge(dots_turned, len(TURNED) * (t - 1))
                    for s in range(GROUP // 2):
                        kept, products = diagonal(t, k, dot, s)
                        last = nc.vector.tensor_copy(kept, products)
                    last.then_inc(dots_set_dve, 1)
                    if t == 0 and HOTS_AMID:
                        one_hot_chunk(hot, k)
                    dot += 1
                if 0 < t < tiles - 1:
                    second_hidden(t - 1)
                if t:
                    dve.wait_ge(pairs_turned, t)
                for bank in (1, 2):
                    dve.wait_ge(dots_turned, len(TURNED) * t + bank + 1)
                    for jb in TURNED[bank]:
                        last = keep_pairs(nc.vector.tensor_copy, jb)
                last.then_inc(by_sample_dve, 1)
                if t:
                    outputs(t - 1)
                if t == 0 and HOTS_AMID:
                    low_part(hot)
                    hot += 1
                for _ in range(HOTS_AFTER[t]):
                    hot_part(hot)
                    hot += 1
            second_hidden(tiles - 1)
            outputs(tiles - 1)


def kernel(r_dense_x, ids, W_top1, b_top1, W_top2, b_top2, W_top3, **tables):
    import numpy as np
    import concourse.bacc as bacc
    from concourse.bass_utils import run_bass_kernel_spmd

    W_top1 = np.asarray(W_top1)
    row_of = np.zeros((TABLES + 1, TABLES + 1), np.int64)
    first, second = np.triu_indices(TABLES + 1, k=1)
    row_of[first, second] = row_of[second, first] = np.arange(len(first))
    w1_pairs = np.zeros((NROW, JR, W_top1.shape[1]), W_top1.dtype)
    for jb in range(JB):
        for jr in range(JR):
            j = jb * JR + jr
            for i in range(j):
                w1_pairs[ROW0[jb] + i, jr] = W_top1[row_of[FEATURES[i], FEATURES[j]]]

    def on_partitions(a):
        return np.asarray(a).reshape(-1, P, *np.asarray(a).shape[1:]).swapaxes(0, 1)

    arrays = {f"tbl_{f}": np.asarray(tables[f"tbl_{f}"]) for f in range(TABLES)}
    arrays |= {
        "ids": np.asarray(ids), "hot_ids": np.asarray(ids).T[[FEATURES[f] for f in HOT]],
        "dense_t": np.asarray(r_dense_x).T, "w1_pairs": w1_pairs,
        "w1_dense": W_top1[len(first):], "b1": on_partitions(b_top1), "w2": on_partitions(W_top2),
        "b2": on_partitions(b_top2), "w3": on_partitions(W_top3)[:, :, 0], "eye": np.eye(P, dtype=np.float32),
    }
    arrays = {f"in_{k}": np.ascontiguousarray(a) for k, a in arrays.items()}
    nc = bacc.Bacc("TRN2", target_bir_lowering=False, num_devices=1)
    ap = {k[3:]: nc.dram_tensor(k, a.shape, mybir.dt.from_np(a.dtype), kind="ExternalInput").ap() for k, a in arrays.items()}
    out = nc.dram_tensor("out_y", (ids.shape[0], 1), F32, kind="ExternalOutput").ap()
    dlrm_tower(nc, ap["ids"], ap["hot_ids"], [ap[f"tbl_{f}"] for f in range(TABLES)], ap["dense_t"], ap["w1_pairs"],
               ap["w1_dense"], ap["b1"], ap["w2"], ap["b2"], ap["w3"], ap["eye"], out)
    return run_bass_kernel_spmd(nc, [arrays], core_ids=[0]).results[0]["out_y"]
```
